# Optimizing a Trainium2 kernel written in Bass

```python
import numpy as np
import jax
import jax.numpy as jnp

def _softmax(x, axis=-1):
    return jax.nn.softmax(x, axis=axis)

def _gelu(x):
    return jax.nn.gelu(x, approximate=True)

def _silu(x):
    return jax.nn.silu(x)

def _sigmoid(x):
    return jax.nn.sigmoid(x)

def _layernorm(x, axis=-1, eps=1e-05):
    m = jnp.mean(x, axis=axis, keepdims=True)
    v = jnp.var(x, axis=axis, keepdims=True)
    return (x - m) / jnp.sqrt(v + eps)

def _scatter_add(tgt, idx, src, axis=0):
    return tgt.at[idx].add(src)

def _segment_sum(src, seg, n):
    return jax.ops.segment_sum(src, seg, n)
kernel_name = 'mk_adj_resnorm_d1_adj_r2_472f15'

def setup_inputs(seed: int=0):
    np.random.seed(seed)
    _w = jnp.asarray

    def _rec_inputs():
        import jax
        import jax.numpy as jnp
        _gk = jax.random.key(seed)
        x = 7.22e-05 + 1 * jax.random.normal(jax.random.fold_in(_gk, 1), (2048, 512), jnp.float32)
        _a = jax.random.bernoulli(jax.random.fold_in(_gk, 2), 0.000976562, (2048, 2048))
        _a = jnp.logical_or(_a, jnp.swapaxes(_a, -1, -2))
        _a = jnp.logical_or(_a, jnp.eye(2048, dtype=bool))
        _af = _a.astype(jnp.float32)
        _d = jnp.maximum(_af.sum(-1), 1.0) ** (-0.5)
        _af = _af * _d[..., :, None] * _d[..., None, :]
        adj = _af
        return (x, adj)
    x, adj = _rec_inputs()

    def _L0_gnn_setup():
        import jax, jax.numpy as jnp
        import numpy as np
        N = 4096
        D = 512

        def adjacent_mat(adj):
            adj = adj + jnp.eye(adj.shape[0], dtype=adj.dtype)
            deg = jnp.sum(adj, axis=1)
            dinv = jnp.where(deg > 0, deg ** (-0.5), 0.0).astype(adj.dtype)
            return dinv[:, None] * adj * dinv[None, :]
        key = jax.random.key(seed)
        k1, k2 = jax.random.split(key)
        x = jax.random.normal(k1, (N, D), dtype=jnp.float32)
        Coefficient2 = 1e-08 * jnp.ones((N, N), dtype=jnp.float32)
        A = jax.random.uniform(k2, (N, N), dtype=jnp.float32)
        return {'x': x, 'Coefficient2': Coefficient2, 'A': A}
    _L0_gnn_all = _L0_gnn_setup()
    _L0_gnn_in = {k: v for k, v in _L0_gnn_all.items() if k in ()}
    del _L0_gnn_all
    return {'x': x, 'adj': adj}

def reference(x, adj):
    import jax
    import jax.numpy as jnp

    def _L0_gnn_ref(x, Coefficient2, A):
        import jax, jax.numpy as jnp
        import numpy as np
        N = 4096
        D = 512

        def adjacent_mat(adj):
            adj = adj + jnp.eye(adj.shape[0], dtype=adj.dtype)
            deg = jnp.sum(adj, axis=1)
            dinv = jnp.where(deg > 0, deg ** (-0.5), 0.0).astype(adj.dtype)
            return dinv[:, None] * adj * dinv[None, :]
        A_c = jax.lax.stop_gradient(A)
        adj = adjacent_mat((A_c + A_c.T) * 0.5)
        y = Coefficient2 @ adj
        y = y @ x
        return y
    x = _layernorm(x + _L0_gnn_ref(x, adj, adj), axis=-1)
    return x

_drawn_inputs = setup_inputs


def setup_inputs(seed=0):
    import zlib

    import numpy as np

    out = dict(_drawn_inputs(seed))
    spreads = {}
    factors = {}
    for name, (base, spread) in spreads.items():
        noise = np.random.default_rng([zlib.crc32(name.encode()), seed]).standard_normal(out[name].shape)
        drawn = base * np.exp(spread * noise) if base else spread * noise
        out[name] = jnp.asarray(drawn.astype(out[name].dtype))
    for name, factor in factors.items():
        out[name] = (out[name] * factor).astype(out[name].dtype)
    return out
```

```python
from contextlib import ExitStack

import concourse.bass as bass
from concourse import mybir

P = 128
F32 = mybir.dt.float32
F32R = mybir.dt.float32r
ALU = mybir.AluOpType
ACT = mybir.ActivationFunctionType

LN_EPS = 1e-5
DEG_MIN = 1e-34
RING_R = 3
BATCH = 4


def gnn_resnorm_kernel(nc: bass.Bass, x: bass.AP, adj: bass.AP, out: bass.AP):
    N, D = x.shape
    NB = N // P
    GROUPS = [range(0, 6), range(6, 11), range(11, 16)]
    assert N == 2048 and D == 512 and GROUPS[-1][-1] == NB - 1
    GW = len(GROUPS[0]) * P
    G1 = len(GROUPS[1])
    HALF = NB // 2

    def batches(j):
        rows = [("row", c, min(BATCH, NB - c)) for c in range(j, NB, BATCH)]
        cols = [("col", r, min(BATCH, NB - r)) for r in range(j + 1, NB, BATCH)]
        return rows + cols

    BATCHES = [batches(j) for j in range(NB)]
    BATCH_BASE = [sum(len(b) for b in BATCHES[:j]) for j in range(NB + 1)]

    with ExitStack() as ctx:
        top = [(nc.sbuf_base + 31) // 32 * 32]

        def at(name, shape, dt, offset):
            return nc.alloc_sbuf_tensor_at(name, [P, *shape], dt, offset=offset)

        def sb(name, shape, dt):
            size = 4
            for n in shape:
                size *= n
            top[0] += (size + 31) // 32 * 32
            return at(name, shape, dt, top[0] - (size + 31) // 32 * 32)

        AT = sb("AT", [NB, N], F32)
        uh_at = top[0]
        UH = sb("UH", [NB, D], F32R)
        ul_at = top[0]
        UL = sb("UL", [NB, D], F32R)
        strip_row = at("strip_row", [RING_R, N], F32, uh_at)
        natural = at("natural", [2, G1 * P], F32, uh_at + 13 * D * 4)
        ux = at("ux", [NB, D], F32, ul_at)
        strip_col = at("strip_col", [2, NB - 1, P], F32, ul_at + 8 * D * 4)

        slots_at = top[0]
        SLOT = 2 * D + 2 * GW
        sb("slots", [2, SLOT], F32)

        def in_slot(name, shape, dt, skip):
            return [at(f"{name}{i}", shape, dt, slots_at + (i * SLOT + skip) * 4) for i in range(2)]

        ZH = in_slot("ZH", [D], F32R, 0)
        ZL = in_slot("ZL", [D], F32R, D)
        MH = in_slot("MH", [GW], F32R, 2 * D)
        ML = in_slot("ML", [GW], F32R, 2 * D + GW)
        ATH = in_slot("ATH", [HALF, P], F32R, 0)
        ATL = in_slot("ATL", [HALF, P], F32R, HALF * P)

        xr = sb("xr", [2, D], F32)
        outr = sb("outr", [2, D], F32)
        ident = sb("ident", [P], F32)
        rowsum = sb("rowsum", [NB], F32)
        deg = sb("deg", [NB], F32)
        degc = sb("degc", [NB], F32)
        mask = sb("mask", [NB], F32)
        root = sb("root", [NB], F32)
        inv = sb("inv", [NB], F32)
        corr = sb("corr", [NB], F32)
        corr2 = sb("corr2", [NB], F32)
        dinv = sb("dinv", [NB], F32)
        dinv_half = sb("dinv_half", [NB], F32)
        dinv_sq = sb("dinv_sq", [NB], F32)
        stats = sb("stats", [2, 6], F32)
        meanvar = sb("meanvar", [2, 2], F32)
        ln = sb("ln", [2, 8], F32)

        banks = [ctx.enter_context(nc.psum_tensor(f"bank{i}", [P, 512], F32)) for i in range(8)]

        def acc(m):
            return banks[m % 8]

        TB = banks[6:8]

        def sem(name):
            return ctx.enter_context(nc.semaphore(name))

        row_in = [sem(f"row_in{i}") for i in range(RING_R)]
        col_in = [sem(f"col_in{i}") for i in range(2)]
        nat_in = [sem(f"nat_in{i}") for i in range(2)]
        x_in = [sem(f"x_in{i}") for i in range(2)]
        ux_in = [sem(f"ux_in{i}") for i in range(3)]
        out_done = [sem(f"out_done{i}") for i in range(2)]
        ident_ready = sem("ident_ready")
        tr_done = sem("tr_done")
        tr_copied = sem("tr_copied")
        msum_done = sem("msum_done")
        deg_chain = sem("deg_chain")
        degc_ready = sem("degc_ready")
        root_done = sem("root_done")
        dinv_ready = sem("dinv_ready")
        mh_done = sem("mh_done")
        ml_done = sem("ml_done")
        zh_done = sem("zh_done")
        zl_done = sem("zl_done")
        prod_done = sem("prod_done")
        ex_done = sem("ex_done")
        u_done = sem("u_done")
        uh_done = sem("uh_done")
        ul_done = sem("ul_done")
        ath_done = sem("ath_done")
        atl_done = sem("atl_done")
        half_done = sem("half_done")
        y_read = sem("y_read")
        ln_chain = sem("ln_chain")
        var_ready = sem("var_ready")
        lroot_done = sem("lroot_done")
        o_ready = sem("o_ready")

        LAST1 = 3 * NB

        def nth(s, slot):
            return 8 * s + (16 - 8 * slot)

        WIDTHS = [len(g) for g in GROUPS]
        PAIRS = [NB * sum(WIDTHS[:g]) for g in range(4)]

        def through(g, k):
            return PAIRS[g] + WIDTHS[g] * (k + 1)

        def complete(g, m):
            return through(g, NB - 2) + m - GROUPS[g][0] + 1

        def block(ap, k):
            return ap[bass.ts(k, P), :]

        ctx_block = ctx.enter_context(nc.Block())

        @ctx_block.sync
        def _(sp):
            def load_x(k, s, slot):
                sp.dma_start(xr[:, slot, :], block(x, k)).then_inc(x_in[slot], 16)

            def load_ux(g, blocks):
                for m in blocks:
                    sp.dma_start(ux[:, m, :], block(x, m)).then_inc(ux_in[g], 16)

            for j in range(NB):
                if j >= RING_R:
                    sp.wait_ge(ml_done, j - RING_R + 1)
                sp.dma_start(strip_row[:, j % RING_R, :], block(adj, j)).then_inc(row_in[j % RING_R], 16)
                if j < NB - 1:
                    if j >= 2:
                        sp.wait_ge(tr_copied, BATCH_BASE[j - 1])
                    sp.dma_start(strip_col[:, j % 2, 0:NB - 1 - j, :],
                                 adj[(j + 1) * P:N, j * P:(j + 1) * P].rearrange("(r p) c -> p r c", p=P)
                                 ).then_inc(col_in[j % 2], 16)
                if j >= 2:
                    sp.wait_ge(zl_done, j - 1)
                load_x(j, j, j % 2)
                if j == 1:
                    load_ux(0, GROUPS[0])

            def load_step(g, k, s, slot, first=False):
                if not first:
                    sp.wait_ge(ml_done, s - 1)
                m0 = GROUPS[g][0]
                sp.dma_start(natural[:, slot, :], block(adj, k)[:, m0 * P:(m0 + G1) * P]
                             ).then_inc(nat_in[slot], 16)
                sp.wait_ge(zl_done, s - 1)
                load_x(k, s, slot)

            for g in (1, 2):
                load_step(g, 0, g * NB, 0, first=g == 1)
                load_step(g, 1, g * NB + 1, 1, first=g == 1)
                sp.wait_ge(tr_copied, BATCH_BASE[NB])
                load_ux(g, GROUPS[g])
                with sp.Fori(1, NB // 2) as i:
                    for slot in range(2):
                        load_step(g, 2 * i + slot, 2 * i + (g * NB + slot), slot)

            sp.wait_ge(zl_done, LAST1 - 1)
            load_x(0, 0, 0)
            sp.wait_ge(zl_done, LAST1)
            load_x(1, 0, 1)

            def store(m, slot):
                sp.wait_ge(o_ready, m + 1)
                sp.dma_start(block(out, m), outr[:, slot, :]).then_inc(out_done[slot], 16)

            with sp.Fori(0, NB // 2 - 1) as i:
                for slot in range(2):
                    store(2 * i + slot, slot)
                    load_x(2 * i + (2 + slot), 0, slot)
            for slot in range(2):
                store(NB - 2 + slot, slot)
            for slot in range(2):
                sp.wait_ge(out_done[slot], 16 * (NB // 2))

        @ctx_block.gpsimd
        def _(pool):
            nc.gpsimd.memset(ident[:, :], 0.0).then_inc(ident_ready, 1)
            pool.wait_ge(ident_ready, 1)
            nc.gpsimd.affine_select(out=ident[:, :], in_=ident[:, :], compare_op=ALU.not_equal, fill=1.0,
                                    base=0, pattern=[[-1, P]], channel_multiplier=1).then_inc(ident_ready, 1)
            with pool.Fori(0, NB) as m:
                pool.wait_ge(uh_done, m + 1)
                one = bass.ds(m, 1)
                nc.gpsimd.tensor_tensor(UL[:, one, :], ux[:, one, :], UH[:, one, :].bitcast(F32), ALU.subtract
                                        ).then_inc(ul_done, 1)

        @ctx_block.scalar
        def _(act):
            def copy_batch(j, n):
                kind, first, count = BATCHES[j][n]
                b = BATCH_BASE[j] + n
                act.wait_ge(tr_done, b + 1)
                src = TB[b % 2][:, 0:count * P]
                if kind == "col":
                    dst = AT[:, j, first * P:(first + count) * P]
                else:
                    dst = AT[:, first:first + count, j * P:(j + 1) * P]
                    src = src.rearrange("p (n c) -> p n c", n=count)
                nc.scalar.activation(dst, src, ACT.Copy).then_inc(tr_copied, 1)

            def z_high(k, s, slot):
                act.wait_ge(x_in[slot], nth(s, slot))
                nc.scalar.activation(ZH[slot][:, :], xr[:, slot, :], ACT.Copy, scale=dinv[:, bass.ds(k, 1)]
                                     ).then_inc(zh_done, 1)

            def ex_scale(m):
                nc.scalar.activation(ux[:, m, :], ux[:, m, :], ACT.Copy, scale=dinv_sq[:, m:m + 1]
                                     ).then_inc(ex_done, 1)

            def u_high(blocks):
                for m in blocks:
                    act.wait_ge(u_done, m + 1)
                    nc.scalar.activation(UH[:, m, :], ux[:, m, :], ACT.Copy).then_inc(uh_done, 1)

            for n in range(len(BATCHES[0])):
                copy_batch(0, n)
            for j in range(NB):
                act.wait_ge(degc_ready, j + 1)
                nc.scalar.activation(root[:, j:j + 1], degc[:, j:j + 1], ACT.Sqrt).then_inc(root_done, 1)
                if j >= 2:
                    act.wait_ge(prod_done, through(0, j - 2))
                act.wait_ge(msum_done, j + 1)
                nc.scalar.activation(MH[j % 2][:, :], strip_row[:, j % RING_R, 0:GW], ACT.Copy
                                     ).then_inc(mh_done, 1)
                nxt = range(len(BATCHES[j + 1])) if j + 1 < NB else range(0)
                for n in nxt[:len(nxt) // 2]:
                    copy_batch(j + 1, n)
                act.wait_ge(dinv_ready, j + 1)
                z_high(j, j, j % 2)
                if j in GROUPS[0]:
                    if j == 0:
                        act.wait_ge(ux_in[0], 16 * len(GROUPS[0]))
                    ex_scale(j)
                for n in nxt[len(nxt) // 2:]:
                    copy_batch(j + 1, n)

            def split_high(g, k, s, slot, before):
                act.wait_ge(prod_done, before)
                z_high(k, s, slot)
                act.wait_ge(msum_done, s + 1)
                nc.scalar.activation(MH[slot][:, 0:G1 * P], natural[:, slot, :], ACT.Copy
                                     ).then_inc(mh_done, 1)

            for g in (1, 2):
                split_high(g, 0, g * NB, 0, through(g - 1, NB - 2))
                u_high(GROUPS[g - 1])
                split_high(g, 1, g * NB + 1, 1, through(g - 1, NB - 1))
                act.wait_ge(ux_in[g], 16 * G1)
                for m in GROUPS[g]:
                    ex_scale(m)
                with act.Fori(1, NB // 2) as i:
                    for slot in range(2):
                        split_high(g, 2 * i + slot, 2 * i + (g * NB + slot), slot,
                                   2 * WIDTHS[g] * i + through(g, slot - 2))

            def half_high(m, h):
                nc.scalar.activation(ATH[h][:, :, :], AT[:, h * HALF:(h + 1) * HALF, bass.ts(m, P)], ACT.Copy
                                     ).then_inc(ath_done, 1)

            def ln_root(m, slot):
                act.wait_ge(var_ready, m + 1)
                nc.scalar.activation(ln[:, slot, 1:2], ln[:, slot, 0:1], ACT.Sqrt).then_inc(lroot_done, 1)

            act.wait_ge(prod_done, through(2, NB - 2))
            half_high(0, 0)
            u_high(GROUPS[2])
            act.wait_ge(prod_done, PAIRS[3])
            half_high(0, 1)

            def columns_high(m, prev_slot):
                for h in range(2):
                    act.wait_ge(half_done, 2 * m + (h - 1))
                    half_high(m, h)
                ln_root(m - 1, prev_slot)

            columns_high(1, 0)
            with act.Fori(1, NB // 2) as i:
                for slot in range(2):
                    columns_high(2 * i + slot, 1 - slot)
            ln_root(NB - 1, 1)

        @ctx_block.vector
        def _(dve):
            def m_low(width, src, s, slot):
                dve.wait_ge(mh_done, s + 1)
                nc.vector.tensor_tensor(ML[slot][:, 0:width], src, MH[slot][:, 0:width].bitcast(F32),
                                        ALU.subtract).then_inc(ml_done, 1)

            def z_low(k, s, slot):
                dve.wait_ge(zh_done, s + 1)
                nc.vector.scalar_tensor_tensor(out=ZL[slot][:, :], in0=xr[:, slot, :],
                                               scalar=dinv[:, bass.ds(k, 1)],
                                               in1=ZH[slot][:, :].bitcast(F32),
                                               op0=ALU.mult, op1=ALU.subtract).then_inc(zl_done, 1)

            LINKS = 7
            for j in range(NB):
                c = slice(j, j + 1)

                def link(ins, n):
                    ins.then_inc(deg_chain, 1)
                    dve.wait_ge(deg_chain, LINKS * j + n)

                dve.wait_ge(tr_copied, BATCH_BASE[j + 1])
                dve.wait_ge(row_in[j % RING_R], 16 * (j // RING_R + 1))
                strip = strip_row[:, j % RING_R, :]
                nc.vector.scalar_tensor_tensor(out=strip, in0=strip, scalar=1.0, in1=AT[:, j, :], op0=ALU.mult,
                                               op1=ALU.add, accum_out=rowsum[:, c]).then_inc(msum_done, 1)
                dve.wait_ge(msum_done, j + 1)
                link(nc.vector.tensor_scalar(deg[:, c], rowsum[:, c], 0.5, 1.0, ALU.mult, ALU.add), 1)
                nc.vector.tensor_scalar(degc[:, c], deg[:, c], DEG_MIN, None, ALU.max).then_inc(degc_ready, 1)
                link(nc.vector.tensor_scalar(mask[:, c], deg[:, c], 0.0, None, ALU.is_gt), 2)
                m_low(GW, strip[:, 0:GW], j, j % 2)
                dve.wait_ge(root_done, j + 1)
                link(nc.vector.reciprocal(inv[:, c], root[:, c]), 3)
                dve.wait_ge(degc_ready, j + 1)
                link(nc.vector.scalar_tensor_tensor(out=corr[:, c], in0=inv[:, c], scalar=degc[:, c], in1=inv[:, c],
                                                    op0=ALU.mult, op1=ALU.mult), 4)
                link(nc.vector.tensor_scalar(corr2[:, c], corr[:, c], -0.5, 1.5, ALU.mult, ALU.add), 5)
                link(nc.vector.tensor_scalar(dinv[:, c], inv[:, c], corr2[:, c], mask[:, c], ALU.mult, ALU.mult), 6)
                nc.vector.tensor_scalar(dinv_half[:, c], dinv[:, c], 0.5, None, ALU.mult).then_inc(deg_chain, 1)
                nc.vector.tensor_tensor(dinv_sq[:, c], dinv[:, c], dinv[:, c], ALU.mult).then_inc(dinv_ready, 1)
                z_low(j, j, j % 2)

            def finish_u(g):
                for m in GROUPS[g]:
                    dve.wait_ge(prod_done, complete(g, m))
                    dve.wait_ge(ex_done, m + 1)
                    nc.vector.scalar_tensor_tensor(out=ux[:, m, :], in0=acc(m)[:, :], scalar=dinv_half[:, m:m + 1],
                                                   in1=ux[:, m, :], op0=ALU.mult, op1=ALU.add).then_inc(u_done, 1)

            def split_low(g, k, s, slot):
                m0 = GROUPS[g][0]
                dve.wait_ge(nat_in[slot], nth(s, slot) - 8 * NB)
                nc.vector.tensor_tensor(natural[:, slot, :], natural[:, slot, :],
                                        AT[:, bass.ds(k, 1), m0 * P:(m0 + G1) * P].rearrange("p o c -> p (o c)"),
                                        ALU.add).then_inc(msum_done, 1)
                z_low(k, s, slot)
                m_low(G1 * P, natural[:, slot, :], s, slot)

            dve.wait_ge(deg_chain, LINKS * NB)
            for g in (1, 2):
                split_low(g, 0, g * NB, 0)
                finish_u(g - 1)
                split_low(g, 1, g * NB + 1, 1)
                with dve.Fori(1, NB // 2) as i:
                    for slot in range(2):
                        split_low(g, 2 * i + slot, 2 * i + (g * NB + slot), slot)

            def half_low(m, h):
                dve.wait_ge(ath_done, 2 * m + (h + 1))
                nc.vector.tensor_tensor(ATL[h][:, :, :], AT[:, h * HALF:(h + 1) * HALF, bass.ts(m, P)],
                                        ATH[h][:, :, :].bitcast(F32), ALU.subtract).then_inc(atl_done, 1)

            LN_LINKS = 6

            def layer_norm(m, slot, first):
                def link(ins, n):
                    ins.then_inc(ln_chain, 1)
                    dve.wait_ge(ln_chain, LN_LINKS * m + n)

                veps, root_, inv_, c1, c2, rstd = (ln[:, slot, n:n + 1] for n in range(6))
                r = xr[:, slot, :]
                dve.wait_ge(half_done, 2 * m + 2)
                dve.wait_ge(x_in[slot], nth(m, slot) + 8 * LAST1)
                nc.vector.tensor_tensor(r, banks[slot][:, :], r, ALU.add).then_inc(y_read, 1)
                dve.wait_ge(y_read, m + 1)
                link(nc.vector.bn_stats(stats[:, slot, :], r), 1)
                nc.vector.memset(veps, LN_EPS)
                link(nc.vector.bn_aggr(meanvar[:, slot, :], stats[:, slot, :]), 2)
                nc.vector.tensor_tensor(veps, meanvar[:, slot, 1:2], veps, ALU.add).then_inc(var_ready, 1)
                dve.wait_ge(lroot_done, m + 1)
                link(nc.vector.reciprocal(inv_, root_), 3)
                link(nc.vector.scalar_tensor_tensor(out=c1, in0=inv_, scalar=veps, in1=inv_,
                                                    op0=ALU.mult, op1=ALU.mult), 4)
                link(nc.vector.tensor_scalar(c2, c1, -0.5, 1.5, ALU.mult, ALU.add), 5)
                link(nc.vector.tensor_scalar(rstd, inv_, c2, None, ALU.mult), 6)
                if not first:
                    dve.wait_ge(out_done[slot], 8 * m - 8 * slot)
                nc.vector.tensor_scalar(outr[:, slot, :], r, meanvar[:, slot, 0:1], rstd, ALU.subtract, ALU.mult
                                        ).then_inc(o_ready, 1)

            half_low(0, 0)
            finish_u(2)
            half_low(0, 1)
            for m in (1, 2, 3):
                half_low(m, 0)
                half_low(m, 1)
                layer_norm(m - 1, (m - 1) % 2, first=m < 3)
            with dve.Fori(2, NB // 2) as i:
                for slot in range(2):
                    half_low(2 * i + slot, 0)
                    half_low(2 * i + slot, 1)
                    layer_norm(2 * i + (slot - 1), 1 - slot, first=False)
            layer_norm(NB - 1, 1, first=False)

        @ctx_block.tensor
        def _(pe):
            def transpose_batch(j, n):
                kind, first, count = BATCHES[j][n]
                b = BATCH_BASE[j] + n
                if n == 0:
                    pe.wait_ge(row_in[j % RING_R], 16 * (j // RING_R + 1))
                if kind == "col" and first == j + 1:
                    pe.wait_ge(col_in[j % 2], 16 * (j // 2 + 1))
                if b >= 2:
                    pe.wait_ge(tr_copied, b - 1)
                for i in range(count):
                    if kind == "row":
                        src = strip_row[:, j % RING_R, (first + i) * P:(first + i + 1) * P]
                    else:
                        src = strip_col[:, j % 2, first + i - j - 1, :]
                    last = nc.tensor.transpose(TB[b % 2][:, i * P:(i + 1) * P], src, ident[:, :])
                last.then_inc(tr_done, 1)

            def products(bank, wh, wl, mh, ml, start, stop):
                nc.tensor.matmul(bank, wh, ml, start=start, stop=False)
                nc.tensor.matmul(bank, wl, mh, start=False, stop=False)
                return nc.tensor.matmul(bank, wh, mh, start=False, stop=stop)

            def contract(group, s, slot, start=False, stop=False, between=None):
                pe.wait_ge(ml_done, s + 1)
                pe.wait_ge(zl_done, s + 1)
                for n, m in enumerate(group):
                    if start and m >= 8:
                        pe.wait_ge(u_done, m - 7)
                    cols = slice(n * P, (n + 1) * P)
                    last = products(acc(m)[:, :], MH[slot][:, cols], ML[slot][:, cols],
                                    ZH[slot][:, :], ZL[slot][:, :], start, stop)
                    last.then_inc(prod_done, 1)
                    if between:
                        between(n)

            pe.wait_ge(ident_ready, 2)
            for j in range(2):
                for n in range(len(BATCHES[j])):
                    transpose_batch(j, n)
            for j in range(NB):
                todo = list(range(len(BATCHES[j + 2]))) if j + 2 < NB else []
                rounds = len(GROUPS[0])

                def between(n):
                    for q in todo[n * len(todo) // rounds:(n + 1) * len(todo) // rounds]:
                        transpose_batch(j + 2, q)

                contract(GROUPS[0], j, j % 2, start=j == 0, stop=j == NB - 1, between=between)

            pe.wait_ge(tr_copied, BATCH_BASE[NB])
            for g in (1, 2):
                group = GROUPS[g]
                contract(group, g * NB, 0, start=True)
                with pe.Fori(0, NB // 2 - 1) as i:
                    for n, slot in ((1, 1), (2, 0)):
                        contract(group, 2 * i + (g * NB + n), slot)
                contract(group, (g + 1) * NB - 1, 1, stop=True)

            def column(m, slot):
                for h in range(2):
                    pe.wait_ge(atl_done, 2 * m + (h + 1))
                    for n in range(HALF):
                        k = h * HALF + n
                        last = products(banks[slot][:, :], ATH[h][:, n, :], ATL[h][:, n, :],
                                        UH[:, k, :], UL[:, k, :], k == 0, k == NB - 1)
                    last.then_inc(half_done, 1)
                    if h == 0:
                        pe.wait_ge(ul_done, NB)

            pe.wait_ge(u_done, GROUPS[2][0] - 1)
            pe.wait_ge(ul_done, HALF)
            column(0, 0)
            column(1, 1)
            with pe.Fori(1, NB // 2) as i:
                for slot in range(2):
                    pe.wait_ge(y_read, 2 * i + (slot - 1))
                    column(2 * i + slot, slot)


def kernel(x, adj):
    import numpy as np
    import concourse.bacc as bacc
    from concourse.bass_utils import run_bass_kernel_spmd

    nc = bacc.Bacc("TRN2", target_bir_lowering=False, num_devices=1, dynamic_dma_scratch_size=1024)
    arrays, args = {}, []
    for name, a in (("x", x), ("adj", adj)):
        a = np.ascontiguousarray(a)
        arrays[f"in_{name}"] = a
        args.append(nc.dram_tensor(f"in_{name}", a.shape, mybir.dt.from_np(a.dtype), kind="ExternalInput").ap())
    args.append(nc.dram_tensor("out_0", x.shape, F32, kind="ExternalOutput").ap())
    gnn_resnorm_kernel(nc, *args)
    r = run_bass_kernel_spmd(nc, [arrays], core_ids=[0])
    return r.results[0]["out_0"]
```

```python
from contextlib import ExitStack

import concourse.bass as bass
from concourse import mybir

P = 128
F32 = mybir.dt.float32
F32R = mybir.dt.float32r
ALU = mybir.AluOpType
ACT = mybir.ActivationFunctionType

LN_EPS = 1e-5
DEG_MIN = 1e-34
RING_R = 4
BATCH = 4
PIECES = 4


def gnn_resnorm_kernel(nc: bass.Bass, x: bass.AP, adj: bass.AP, out: bass.AP):
    N, D = x.shape
    NB = N // P
    GROUPS = [range(0, 6), range(6, 11), range(11, 16)]
    assert N == 2048 and D == 512 and GROUPS[-1][-1] == NB - 1
    GW = len(GROUPS[0]) * P
    G1 = len(GROUPS[1])
    UX_STEP = NB - len(GROUPS[0])
    HALF = NB // 2

    def batches(j):
        rows = [("row", c, min(BATCH, NB - c)) for c in range(j, NB, BATCH)]
        cols = [("col", r, min(BATCH, NB - r)) for r in range(j + 1, NB, BATCH)]
        return rows + cols

    BATCHES = [batches(j) for j in range(NB)]
    BATCH_BASE = [sum(len(b) for b in BATCHES[:j]) for j in range(NB + 1)]

    AHEAD = 4
    STRIPS = [[2], [3], [4, 5]] + [[j + 3] if j + 3 < NB else [] for j in range(3, NB)]

    def between_products(j):
        return [(i, n) for i in STRIPS[j] for n in range(len(BATCHES[i]))] if j >= 0 else []

    with ExitStack() as ctx:
        top = [(nc.sbuf_base + 31) // 32 * 32]

        def at(name, shape, dt, offset):
            return nc.alloc_sbuf_tensor_at(name, [P, *shape], dt, offset=offset)

        def sb(name, shape, dt):
            size = 4
            for n in shape:
                size *= n
            top[0] += (size + 31) // 32 * 32
            return at(name, shape, dt, top[0] - (size + 31) // 32 * 32)

        AT = sb("AT", [NB, N], F32)
        uh_at = top[0]
        UH = sb("UH", [NB, D], F32R)
        ul_at = top[0]
        UL = sb("UL", [NB, D], F32R)
        strip_row = at("strip_row", [RING_R, N], F32, uh_at)
        ux = at("ux", [NB, D], F32, ul_at)
        strip_col = at("strip_col", [2, NB - 1, P], F32, ul_at + 8 * D * 4)

        slots_at = top[0]
        SLOT = 2 * D + 2 * GW
        sb("slots", [2, SLOT], F32)

        def in_slot(name, shape, dt, skip):
            return [at(f"{name}{i}", shape, dt, slots_at + (i * SLOT + skip) * 4) for i in range(2)]

        ZH = in_slot("ZH", [D], F32R, 0)
        ZL = in_slot("ZL", [D], F32R, D)
        MH = in_slot("MH", [GW], F32R, 2 * D)
        ML = in_slot("ML", [GW], F32R, 2 * D + GW)
        ATH = in_slot("ATH", [HALF, P], F32R, 0)
        ATL = in_slot("ATL", [HALF, P], F32R, HALF * P)

        xr = sb("xr", [2, D], F32)
        outr = sb("outr", [2, D], F32)
        natural = [at("natural0", [G1 * P], F32, top[0] - 2 * D * 4),
                   at("natural1", [G1 * P], F32, uh_at + 13 * D * 4)]
        ident = sb("ident", [P], F32)
        rowsum = sb("rowsum", [NB], F32)
        deg = sb("deg", [NB], F32)
        degc = sb("degc", [NB], F32)
        mask = sb("mask", [NB], F32)
        root = sb("root", [NB], F32)
        inv = sb("inv", [NB], F32)
        corr = sb("corr", [NB], F32)
        corr2 = sb("corr2", [NB], F32)
        dinv = sb("dinv", [NB], F32)
        dinv_half = sb("dinv_half", [NB], F32)
        dinv_sq = sb("dinv_sq", [NB], F32)
        stats = sb("stats", [2, 6], F32)
        meanvar = sb("meanvar", [2, 2], F32)
        ln = sb("ln", [2, 8], F32)

        banks = [ctx.enter_context(nc.psum_tensor(f"bank{i}", [P, 512], F32)) for i in range(8)]

        def acc(m):
            return banks[m % 8]

        TB = banks[6:8]

        def sem(name):
            return ctx.enter_context(nc.semaphore(name))

        piece_in = [sem(f"piece_in{i}") for i in range(PIECES)]
        row_in = [sem(f"row_in{i}") for i in range(RING_R)]
        col_in = [sem(f"col_in{i}") for i in range(2)]
        nat_in = [sem(f"nat_in{i}") for i in range(2)]
        x_in = [sem(f"x_in{i}") for i in range(2)]
        ux_in = [sem(f"ux_in{i}") for i in range(3)]
        out_done = [sem(f"out_done{i}") for i in range(2)]
        ident_ready = sem("ident_ready")
        tr_done = sem("tr_done")
        tr_copied = sem("tr_copied")
        msum_done = sem("msum_done")
        deg_chain = sem("deg_chain")
        degc_ready = sem("degc_ready")
        root_done = sem("root_done")
        dinv_ready = sem("dinv_ready")
        mh_done = sem("mh_done")
        ml_done = sem("ml_done")
        zh_done = sem("zh_done")
        zl_done = sem("zl_done")
        prod_done = sem("prod_done")
        ex_done = sem("ex_done")
        u_done = sem("u_done")
        uh_done = sem("uh_done")
        ul_done = sem("ul_done")
        ath_done = sem("ath_done")
        atl_done = sem("atl_done")
        half_done = sem("half_done")
        y_read = sem("y_read")
        ln_chain = sem("ln_chain")
        var_ready = sem("var_ready")
        lroot_done = sem("lroot_done")
        o_ready = sem("o_ready")

        LAST1 = 3 * NB

        def row_nth(j):
            return 16 * (j // RING_R + (j % RING_R > 0))

        def nth(s, slot):
            return 8 * s + (16 - 8 * slot)

        WIDTHS = [len(g) for g in GROUPS]
        PAIRS = [NB * sum(WIDTHS[:g]) for g in range(4)]

        def through(g, k):
            return PAIRS[g] + WIDTHS[g] * (k + 1)

        def complete(g, m):
            return through(g, NB - 2) + m - GROUPS[g][0] + 1

        def block(ap, k):
            return ap[bass.ts(k, P), :]

        ctx_block = ctx.enter_context(nc.Block())

        @ctx_block.sync
        def _(sp):
            def load_x(k, s, slot):
                sp.dma_start(xr[:, slot, :], block(x, k)).then_inc(x_in[slot], 16)

            def load_ux(g, blocks):
                for m in blocks:
                    sp.dma_start(ux[:, m, :], block(x, m)).then_inc(ux_in[g], 16)

            def load_rows(j):
                if j >= RING_R:
                    sp.wait_ge(ml_done, j - RING_R + 1)
                if j == 0:
                    for n in range(PIECES):
                        cols = slice(n * N // PIECES, (n + 1) * N // PIECES)
                        sp.dma_start(strip_row[:, 0, cols], block(adj, 0)[:, cols]).then_inc(piece_in[n], 16)
                else:
                    sp.dma_start(strip_row[:, j % RING_R, :], block(adj, j)).then_inc(row_in[j % RING_R], 16)

            def load_cols(j):
                if j >= 2:
                    sp.wait_ge(tr_copied, BATCH_BASE[j - 1])
                sp.dma_start(strip_col[:, j % 2, 0:NB - 1 - j, :],
                             adj[(j + 1) * P:N, j * P:(j + 1) * P].rearrange("(r p) c -> p r c", p=P)
                             ).then_inc(col_in[j % 2], 16)

            for j in range(RING_R):
                load_rows(j)
                load_cols(j)
                if j < 2:
                    load_x(j, j, j)
            for j in range(2, NB):
                if j + 2 < NB:
                    load_rows(j + 2)
                sp.wait_ge(zl_done, j - 1)
                load_x(j, j, j % 2)
                if j + 2 < NB - 1:
                    load_cols(j + 2)
                if j == UX_STEP - 2:
                    load_ux(0, GROUPS[0])

            def load_step(g, k, s, slot):
                sp.wait_ge(ml_done, s - 1)
                m0 = GROUPS[g][0]
                sp.dma_start(natural[slot][:, :], block(adj, k)[:, m0 * P:(m0 + G1) * P]
                             ).then_inc(nat_in[slot], 16)
                sp.wait_ge(zl_done, s - 1)
                load_x(k, s, slot)

            for g in (1, 2):
                load_step(g, 0, g * NB, 0)
                load_step(g, 1, g * NB + 1, 1)
                sp.wait_ge(tr_copied, BATCH_BASE[NB])
                load_ux(g, GROUPS[g])
                with sp.Fori(1, NB // 2) as i:
                    for slot in range(2):
                        load_step(g, 2 * i + slot, 2 * i + (g * NB + slot), slot)

            sp.wait_ge(zl_done, LAST1 - 1)
            load_x(0, 0, 0)
            sp.wait_ge(zl_done, LAST1)
            load_x(1, 0, 1)

            def store(m, slot):
                sp.wait_ge(o_ready, m + 1)
                sp.dma_start(block(out, m), outr[:, slot, :]).then_inc(out_done[slot], 16)

            with sp.Fori(0, NB // 2 - 1) as i:
                for slot in range(2):
                    store(2 * i + slot, slot)
                    load_x(2 * i + (2 + slot), 0, slot)
            for slot in range(2):
                store(NB - 2 + slot, slot)
            for slot in range(2):
                sp.wait_ge(out_done[slot], 16 * (NB // 2))

        @ctx_block.gpsimd
        def _(pool):
            nc.gpsimd.memset(ident[:, :], 0.0).then_inc(ident_ready, 1)
            pool.wait_ge(ident_ready, 1)
            nc.gpsimd.affine_select(out=ident[:, :], in_=ident[:, :], compare_op=ALU.not_equal, fill=1.0,
                                    base=0, pattern=[[-1, P]], channel_multiplier=1).then_inc(ident_ready, 1)
            with pool.Fori(0, NB) as m:
                pool.wait_ge(uh_done, m + 1)
                one = bass.ds(m, 1)
                nc.gpsimd.tensor_tensor(UL[:, one, :], ux[:, one, :], UH[:, one, :].bitcast(F32), ALU.subtract
                                        ).then_inc(ul_done, 1)

        @ctx_block.scalar
        def _(act):
            def copy_batch(j, n):
                kind, first, count = BATCHES[j][n]
                b = BATCH_BASE[j] + n
                act.wait_ge(tr_done, b + 1)
                src = TB[b % 2][:, 0:count * P]
                if kind == "col":
                    dst = AT[:, j, first * P:(first + count) * P]
                else:
                    dst = AT[:, first:first + count, j * P:(j + 1) * P]
                    src = src.rearrange("p (n c) -> p n c", n=count)
                nc.scalar.activation(dst, src, ACT.Copy).then_inc(tr_copied, 1)

            def z_high(k, s, slot):
                act.wait_ge(x_in[slot], nth(s, slot))
                nc.scalar.activation(ZH[slot][:, :], xr[:, slot, :], ACT.Copy, scale=dinv[:, bass.ds(k, 1)]
                                     ).then_inc(zh_done, 1)

            def ex_scale(m):
                nc.scalar.activation(ux[:, m, :], ux[:, m, :], ACT.Copy, scale=dinv_sq[:, m:m + 1]
                                     ).then_inc(ex_done, 1)

            def u_high(blocks):
                for m in blocks:
                    act.wait_ge(u_done, m + 1)
                    nc.scalar.activation(UH[:, m, :], ux[:, m, :], ACT.Copy).then_inc(uh_done, 1)

            def degree_root(j):
                act.wait_ge(degc_ready, j + 1)
                nc.scalar.activation(root[:, j:j + 1], degc[:, j:j + 1], ACT.Sqrt).then_inc(root_done, 1)

            for j in range(2):
                for n in range(len(BATCHES[j])):
                    copy_batch(j, n)
                if j == 0:
                    degree_root(0)
            for j in range(NB):
                if 0 < j <= AHEAD:
                    degree_root(j)
                if j >= 2:
                    act.wait_ge(prod_done, through(0, j - 2))
                act.wait_ge(msum_done, j + 1)
                nc.scalar.activation(MH[j % 2][:, :], strip_row[:, j % RING_R, 0:GW], ACT.Copy
                                     ).then_inc(mh_done, 1)
                act.wait_ge(dinv_ready, j + 1)
                z_high(j, j, j % 2)
                todo = between_products(j - 1)
                for i, n in todo[:2]:
                    copy_batch(i, n)
                if AHEAD <= j < NB - 1:
                    degree_root(j + 1)
                for i, n in todo[2:]:
                    copy_batch(i, n)
                if j >= UX_STEP:
                    if j == UX_STEP:
                        act.wait_ge(ux_in[0], 16 * len(GROUPS[0]))
                    ex_scale(j - UX_STEP)

            def split_high(g, k, s, slot, before):
                act.wait_ge(prod_done, before)
                z_high(k, s, slot)
                act.wait_ge(msum_done, s + 1)
                nc.scalar.activation(MH[slot][:, 0:G1 * P], natural[slot][:, :], ACT.Copy
                                     ).then_inc(mh_done, 1)

            for g in (1, 2):
                split_high(g, 0, g * NB, 0, through(g - 1, NB - 2))
                u_high(GROUPS[g - 1])
                split_high(g, 1, g * NB + 1, 1, through(g - 1, NB - 1))
                act.wait_ge(ux_in[g], 16 * G1)
                for m in GROUPS[g]:
                    ex_scale(m)
                with act.Fori(1, NB // 2) as i:
                    for slot in range(2):
                        split_high(g, 2 * i + slot, 2 * i + (g * NB + slot), slot,
                                   2 * WIDTHS[g] * i + through(g, slot - 2))

            def half_high(m, h):
                nc.scalar.activation(ATH[h][:, :, :], AT[:, h * HALF:(h + 1) * HALF, bass.ts(m, P)], ACT.Copy
                                     ).then_inc(ath_done, 1)

            def ln_root(m, slot):
                act.wait_ge(var_ready, m + 1)
                nc.scalar.activation(ln[:, slot, 1:2], ln[:, slot, 0:1], ACT.Sqrt).then_inc(lroot_done, 1)

            act.wait_ge(prod_done, through(2, NB - 2))
            half_high(0, 0)
            u_high(GROUPS[2])
            act.wait_ge(prod_done, PAIRS[3])
            half_high(0, 1)

            def columns_high(m, prev_slot):
                for h in range(2):
                    act.wait_ge(half_done, 2 * m + (h - 1))
                    half_high(m, h)
                ln_root(m - 1, prev_slot)

            columns_high(1, 0)
            with act.Fori(1, NB // 2) as i:
                for slot in range(2):
                    columns_high(2 * i + slot, 1 - slot)
            ln_root(NB - 1, 1)

        @ctx_block.vector
        def _(dve):
            def m_low(width, src, s, slot):
                dve.wait_ge(mh_done, s + 1)
                nc.vector.tensor_tensor(ML[slot][:, 0:width], src, MH[slot][:, 0:width].bitcast(F32),
                                        ALU.subtract).then_inc(ml_done, 1)

            def z_low(k, s, slot):
                dve.wait_ge(zh_done, s + 1)
                nc.vector.scalar_tensor_tensor(out=ZL[slot][:, :], in0=xr[:, slot, :],
                                               scalar=dinv[:, bass.ds(k, 1)],
                                               in1=ZH[slot][:, :].bitcast(F32),
                                               op0=ALU.mult, op1=ALU.subtract).then_inc(zl_done, 1)

            LINKS = 7
            def link(ins, j, n):
                ins.then_inc(deg_chain, 1)
                dve.wait_ge(deg_chain, LINKS * j + n)

            def row_sums(j):
                c = slice(j, j + 1)
                dve.wait_ge(tr_copied, BATCH_BASE[j + 1])
                if j > 0:
                    dve.wait_ge(row_in[j % RING_R], row_nth(j))
                strip = strip_row[:, j % RING_R, :]
                nc.vector.scalar_tensor_tensor(out=strip, in0=strip, scalar=1.0, in1=AT[:, j, :], op0=ALU.mult,
                                               op1=ALU.add, accum_out=rowsum[:, c]).then_inc(msum_done, 1)
                dve.wait_ge(msum_done, j + 1)
                link(nc.vector.tensor_scalar(deg[:, c], rowsum[:, c], 0.5, 1.0, ALU.mult, ALU.add), j, 1)
                nc.vector.tensor_scalar(degc[:, c], deg[:, c], DEG_MIN, None, ALU.max).then_inc(degc_ready, 1)
                nc.vector.tensor_scalar(mask[:, c], deg[:, c], 0.0, None, ALU.is_gt).then_inc(deg_chain, 1)

            def degree(j):
                c = slice(j, j + 1)
                dve.wait_ge(root_done, j + 1)
                link(nc.vector.reciprocal(inv[:, c], root[:, c]), j, 3)
                dve.wait_ge(degc_ready, j + 1)
                link(nc.vector.scalar_tensor_tensor(out=corr[:, c], in0=inv[:, c], scalar=degc[:, c], in1=inv[:, c],
                                                    op0=ALU.mult, op1=ALU.mult), j, 4)
                link(nc.vector.tensor_scalar(corr2[:, c], corr[:, c], -0.5, 1.5, ALU.mult, ALU.add), j, 5)
                link(nc.vector.tensor_scalar(dinv[:, c], inv[:, c], corr2[:, c], mask[:, c], ALU.mult, ALU.mult), j, 6)
                nc.vector.tensor_tensor(dinv_sq[:, c], dinv[:, c], dinv[:, c], ALU.mult).then_inc(dinv_ready, 1)
                nc.vector.tensor_scalar(dinv_half[:, c], dinv[:, c], 0.5, None, ALU.mult).then_inc(deg_chain, 1)

            for j in range(NB):
                if j <= AHEAD:
                    row_sums(j)
                    degree(j)
                ahead = AHEAD <= j < NB - 1
                if ahead:
                    row_sums(j + 1)
                m_low(GW, strip_row[:, j % RING_R, 0:GW], j, j % 2)
                z_low(j, j, j % 2)
                if ahead:
                    degree(j + 1)

            def finish_u(g):
                for m in GROUPS[g]:
                    dve.wait_ge(prod_done, complete(g, m))
                    dve.wait_ge(ex_done, m + 1)
                    nc.vector.scalar_tensor_tensor(out=ux[:, m, :], in0=acc(m)[:, :], scalar=dinv_half[:, m:m + 1],
                                                   in1=ux[:, m, :], op0=ALU.mult, op1=ALU.add).then_inc(u_done, 1)

            def split_low(g, k, s, slot):
                m0 = GROUPS[g][0]
                dve.wait_ge(nat_in[slot], nth(s, slot) - 8 * NB)
                nc.vector.tensor_tensor(natural[slot][:, :], natural[slot][:, :],
                                        AT[:, bass.ds(k, 1), m0 * P:(m0 + G1) * P].rearrange("p o c -> p (o c)"),
                                        ALU.add).then_inc(msum_done, 1)
                z_low(k, s, slot)
                m_low(G1 * P, natural[slot][:, :], s, slot)

            dve.wait_ge(deg_chain, LINKS * NB)
            for g in (1, 2):
                split_low(g, 0, g * NB, 0)
                finish_u(g - 1)
                split_low(g, 1, g * NB + 1, 1)
                with dve.Fori(1, NB // 2) as i:
                    for slot in range(2):
                        split_low(g, 2 * i + slot, 2 * i + (g * NB + slot), slot)

            def half_low(m, h):
                dve.wait_ge(ath_done, 2 * m + (h + 1))
                nc.vector.tensor_tensor(ATL[h][:, :, :], AT[:, h * HALF:(h + 1) * HALF, bass.ts(m, P)],
                                        ATH[h][:, :, :].bitcast(F32), ALU.subtract).then_inc(atl_done, 1)

            LN_LINKS = 6

            def layer_norm(m, slot, first):
                def link(ins, n):
                    ins.then_inc(ln_chain, 1)
                    dve.wait_ge(ln_chain, LN_LINKS * m + n)

                veps, root_, inv_, c1, c2, rstd = (ln[:, slot, n:n + 1] for n in range(6))
                r = xr[:, slot, :]
                dve.wait_ge(half_done, 2 * m + 2)
                dve.wait_ge(x_in[slot], nth(m, slot) + 8 * LAST1)
                nc.vector.tensor_tensor(r, banks[slot][:, :], r, ALU.add).then_inc(y_read, 1)
                dve.wait_ge(y_read, m + 1)
                link(nc.vector.bn_stats(stats[:, slot, :], r), 1)
                nc.vector.memset(veps, LN_EPS)
                link(nc.vector.bn_aggr(meanvar[:, slot, :], stats[:, slot, :]), 2)
                nc.vector.tensor_tensor(veps, meanvar[:, slot, 1:2], veps, ALU.add).then_inc(var_ready, 1)
                dve.wait_ge(lroot_done, m + 1)
                link(nc.vector.reciprocal(inv_, root_), 3)
                link(nc.vector.scalar_tensor_tensor(out=c1, in0=inv_, scalar=veps, in1=inv_,
                                                    op0=ALU.mult, op1=ALU.mult), 4)
                link(nc.vector.tensor_scalar(c2, c1, -0.5, 1.5, ALU.mult, ALU.add), 5)
                link(nc.vector.tensor_scalar(rstd, inv_, c2, None, ALU.mult), 6)
                if not first:
                    dve.wait_ge(out_done[slot], 8 * m - 8 * slot)
                nc.vector.tensor_scalar(outr[:, slot, :], r, meanvar[:, slot, 0:1], rstd, ALU.subtract, ALU.mult
                                        ).then_inc(o_ready, 1)

            half_low(0, 0)
            finish_u(2)
            half_low(0, 1)
            for m in (1, 2, 3):
                half_low(m, 0)
                half_low(m, 1)
                layer_norm(m - 1, (m - 1) % 2, first=m < 3)
            with dve.Fori(2, NB // 2) as i:
                for slot in range(2):
                    half_low(2 * i + slot, 0)
                    half_low(2 * i + slot, 1)
                    layer_norm(2 * i + (slot - 1), 1 - slot, first=False)
            layer_norm(NB - 1, 1, first=False)

        @ctx_block.tensor
        def _(pe):
            def transpose_batch(j, n):
                kind, first, count = BATCHES[j][n]
                b = BATCH_BASE[j] + n
                if j == 0 and kind == "row":
                    pe.wait_ge(piece_in[first // BATCH], 16)
                elif n == 0:
                    pe.wait_ge(row_in[j % RING_R], row_nth(j))
                if kind == "col" and first == j + 1:
                    pe.wait_ge(col_in[j % 2], 16 * (j // 2 + 1))
                if b >= 2:
                    pe.wait_ge(tr_copied, b - 1)
                for i in range(count):
                    if kind == "row":
                        src = strip_row[:, j % RING_R, (first + i) * P:(first + i + 1) * P]
                    else:
                        src = strip_col[:, j % 2, first + i - j - 1, :]
                    last = nc.tensor.transpose(TB[b % 2][:, i * P:(i + 1) * P], src, ident[:, :])
                last.then_inc(tr_done, 1)

            def products(bank, wh, wl, mh, ml, start, stop):
                nc.tensor.matmul(bank, wh, ml, start=start, stop=False)
                nc.tensor.matmul(bank, wl, mh, start=False, stop=False)
                return nc.tensor.matmul(bank, wh, mh, start=False, stop=stop)

            def contract(group, s, slot, start=False, stop=False, between=None):
                pe.wait_ge(ml_done, s + 1)
                pe.wait_ge(zl_done, s + 1)
                for n, m in enumerate(group):
                    if start and m >= 8:
                        pe.wait_ge(u_done, m - 7)
                    cols = slice(n * P, (n + 1) * P)
                    last = products(acc(m)[:, :], MH[slot][:, cols], ML[slot][:, cols],
                                    ZH[slot][:, :], ZL[slot][:, :], start, stop)
                    last.then_inc(prod_done, 1)
                    if between:
                        between(n)

            pe.wait_ge(ident_ready, 2)
            for j in range(2):
                for n in range(len(BATCHES[j])):
                    transpose_batch(j, n)
            for j in range(NB):
                todo = between_products(j)
                if j < AHEAD - 1:
                    rounds = [[]] * 5 + [todo]
                else:
                    cuts = [q * len(todo) // 5 for q in range(6)]
                    rounds = [[]] + [todo[p:q] for p, q in zip(cuts, cuts[1:])]

                def between(n):
                    for i, q in rounds[n]:
                        transpose_batch(i, q)

                contract(GROUPS[0], j, j % 2, start=j == 0, stop=j == NB - 1, between=between)

            pe.wait_ge(tr_copied, BATCH_BASE[NB])
            for g in (1, 2):
                group = GROUPS[g]
                contract(group, g * NB, 0, start=True)
                with pe.Fori(0, NB // 2 - 1) as i:
                    for n, slot in ((1, 1), (2, 0)):
                        contract(group, 2 * i + (g * NB + n), slot)
                contract(group, (g + 1) * NB - 1, 1, stop=True)

            def column(m, slot):
                for h in range(2):
                    pe.wait_ge(atl_done, 2 * m + (h + 1))
                    for n in range(HALF):
                        k = h * HALF + n
                        last = products(banks[slot][:, :], ATH[h][:, n, :], ATL[h][:, n, :],
                                        UH[:, k, :], UL[:, k, :], k == 0, k == NB - 1)
                    last.then_inc(half_done, 1)
                    if h == 0:
                        pe.wait_ge(ul_done, NB)

            pe.wait_ge(u_done, GROUPS[2][0] - 1)
            pe.wait_ge(ul_done, HALF)
            column(0, 0)
            column(1, 1)
            with pe.Fori(1, NB // 2) as i:
                for slot in range(2):
                    pe.wait_ge(y_read, 2 * i + (slot - 1))
                    column(2 * i + slot, slot)


def kernel(x, adj):
    import numpy as np
    import concourse.bacc as bacc
    from concourse.bass_utils import run_bass_kernel_spmd

    nc = bacc.Bacc("TRN2", target_bir_lowering=False, num_devices=1, dynamic_dma_scratch_size=1024)
    arrays, args = {}, []
    for name, a in (("x", x), ("adj", adj)):
        a = np.ascontiguousarray(a)
        arrays[f"in_{name}"] = a
        args.append(nc.dram_tensor(f"in_{name}", a.shape, mybir.dt.from_np(a.dtype), kind="ExternalInput").ap())
    args.append(nc.dram_tensor("out_0", x.shape, F32, kind="ExternalOutput").ap())
    gnn_resnorm_kernel(nc, *args)
    r = run_bass_kernel_spmd(nc, [arrays], core_ids=[0])
    return r.results[0]["out_0"]
```

```python
from contextlib import ExitStack

import concourse.bass as bass
from concourse import mybir

P = 128
F32 = mybir.dt.float32
F32R = mybir.dt.float32r
ALU = mybir.AluOpType
ACT = mybir.ActivationFunctionType

LN_EPS = 1e-5
DEG_MIN = 1e-34
RING_R = 4
BATCH = 4
PIECES = 4


def gnn_resnorm_kernel(nc: bass.Bass, x: bass.AP, adj: bass.AP, out: bass.AP):
    N, D = x.shape
    NB = N // P
    GROUPS = [range(0, 6), range(6, 11), range(11, 16)]
    assert N == 2048 and D == 512 and GROUPS[-1][-1] == NB - 1
    GW = len(GROUPS[0]) * P
    G1 = len(GROUPS[1])
    UX_STEP = NB // 2
    HALF = NB // 2

    def batches(j):
        rows = [("row", c, min(BATCH, NB - c)) for c in range(j, NB, BATCH)]
        cols = [("col", r, min(BATCH, NB - r)) for r in range(j + 1, NB, BATCH)]
        return rows + cols

    BATCHES = [batches(j) for j in range(NB)]
    BATCH_BASE = [sum(len(b) for b in BATCHES[:j]) for j in range(NB + 1)]

    STRIPS = [[2], [3], [4, 5]] + [[j + 3] if j + 3 < NB else [] for j in range(3, NB)]
    AHEAD = 4
    FIRST_ROUND = [0, 0, 0, 2, 2]
    COPIES_FOR_SUM = [4, 2, 4, 3, 0]
    COPIES_FOR_D = [1, 2, 0, 2, 2, 0]

    def between_products(j):
        return [(i, n) for i in STRIPS[j] for n in range(len(BATCHES[i]))] 

    with ExitStack() as ctx:
        top = [(nc.sbuf_base + 31) // 32 * 32]

        def at(name, shape, dt, offset):
            return nc.alloc_sbuf_tensor_at(name, [P, *shape], dt, offset=offset)

        def sb(name, shape, dt):
            size = 4
            for n in shape:
                size *= n
            top[0] += (size + 31) // 32 * 32
            return at(name, shape, dt, top[0] - (size + 31) // 32 * 32)

        AT = sb("AT", [NB, N], F32)
        uh_at = top[0]
        UH = sb("UH", [NB, D], F32R)
        ul_at = top[0]
        UL = sb("UL", [NB, D], F32R)
        strip_row = at("strip_row", [RING_R, N], F32, uh_at)
        ux = at("ux", [NB, D], F32, ul_at)
        strip_col = at("strip_col", [2, NB - 1, P], F32, ul_at + 8 * D * 4)

        slots_at = top[0]
        SLOT = 2 * D + 2 * GW
        sb("slots", [2, SLOT], F32)

        def in_slot(name, shape, dt, skip):
            return [at(f"{name}{i}", shape, dt, slots_at + (i * SLOT + skip) * 4) for i in range(2)]

        ZH = in_slot("ZH", [D], F32R, 0)
        ZL = in_slot("ZL", [D], F32R, D)
        MH = in_slot("MH", [GW], F32R, 2 * D)
        ML = in_slot("ML", [GW], F32R, 2 * D + GW)
        ATH = in_slot("ATH", [HALF, P], F32R, 0)
        ATL = in_slot("ATL", [HALF, P], F32R, HALF * P)

        xr = sb("xr", [2, D], F32)
        outr = sb("outr", [2, D], F32)
        natural = [at("natural0", [G1 * P], F32, top[0] - 2 * D * 4),
                   at("natural1", [G1 * P], F32, uh_at + 13 * D * 4)]
        ident = sb("ident", [P], F32)
        rowsum = sb("rowsum", [NB], F32)
        deg = sb("deg", [NB], F32)
        degc = sb("degc", [NB], F32)
        deg_neg = sb("deg_neg", [NB], F32)
        mask = sb("mask", [NB], F32)
        root = sb("root", [NB], F32)
        inv = sb("inv", [NB], F32)
        corr = sb("corr", [NB], F32)
        corr2 = sb("corr2", [NB], F32)
        dinv_open = sb("dinv_open", [NB], F32)
        dinv = sb("dinv", [NB], F32)
        dinv_half = sb("dinv_half", [NB], F32)
        partial = sb("partial", [4], F32)
        spare = sb("spare", [1], F32)
        stats = sb("stats", [2, 6], F32)
        meanvar = sb("meanvar", [2, 2], F32)
        ln = sb("ln", [2, 8], F32)

        banks = [ctx.enter_context(nc.psum_tensor(f"bank{i}", [P, 512], F32)) for i in range(8)]

        def acc(m):
            return banks[m % 8]

        TB = banks[6:8]

        def sem(name):
            return ctx.enter_context(nc.semaphore(name))

        piece_in = [sem(f"piece_in{i}") for i in range(2 * PIECES)]
        row_in = [sem(f"row_in{i}") for i in range(RING_R)]
        col_in = [sem(f"col_in{i}") for i in range(2)]
        nat_in = [sem(f"nat_in{i}") for i in range(2)]
        x_in = [sem(f"x_in{i}") for i in range(2)]
        ux_in = [sem(f"ux_in{i}") for i in range(3)]
        out_done = [sem(f"out_done{i}") for i in range(2)]
        ident_ready = sem("ident_ready")
        tr_done = sem("tr_done")
        tr_copied = sem("tr_copied")
        msum_done = sem("msum_done")
        partial_done = sem("partial_done")
        PIECEWISE = 4
        PARTS = [sum(sum(kind == "col" for kind, _, _ in b) for b in BATCHES[:j]) for j in range(PIECEWISE + 1)]
        deg_done = sem("deg_done")
        newton_chain = sem("newton_chain")
        half_ready = sem("half_ready")
        degc_ready = sem("degc_ready")
        root_done = sem("root_done")
        inv_done = sem("inv_done")
        dinv_ready = sem("dinv_ready")
        mh_done = sem("mh_done")
        ml_done = sem("ml_done")
        zh_done = sem("zh_done")
        zl_done = sem("zl_done")
        prod_done = sem("prod_done")
        ex_done = sem("ex_done")
        u_done = sem("u_done")
        uh_done = sem("uh_done")
        ul_done = sem("ul_done")
        ath_done = sem("ath_done")
        atl_done = sem("atl_done")
        half_done = sem("half_done")
        y_read = sem("y_read")
        ln_chain = sem("ln_chain")
        var_ready = sem("var_ready")
        lroot_done = sem("lroot_done")
        o_ready = sem("o_ready")

        LAST1 = 3 * NB

        def row_nth(j):
            return 16 * (j // RING_R + (j % RING_R > 0))

        def col_nth(j):
            return 16 * ((j + 1) // 2)

        def nth(s, slot):
            return 8 * s + (16 - 8 * slot)

        WIDTHS = [len(g) for g in GROUPS]
        PAIRS = [NB * sum(WIDTHS[:g]) for g in range(4)]

        def through(g, k):
            return PAIRS[g] + WIDTHS[g] * (k + 1)

        def complete(g, m):
            return through(g, NB - 2) + m - GROUPS[g][0] + 1

        def degree(j, engine, scaled):
            c = slice(j, j + 1)
            engine.wait_ge(inv_done, j + 1)
            scaled(corr[:, c], inv[:, c], deg_neg[:, c], 0.0).then_inc(newton_chain, 1)
            engine.wait_ge(newton_chain, 3 * j + 1)
            scaled(corr2[:, c], corr[:, c], inv[:, c], 1.5).then_inc(newton_chain, 1)
            engine.wait_ge(newton_chain, 3 * j + 2)
            scaled(dinv_open[:, c], corr2[:, c], inv[:, c], 0.0).then_inc(newton_chain, 1)
            engine.wait_ge(newton_chain, 3 * j + 3)
            scaled(dinv[:, c], dinv_open[:, c], mask[:, c], 0.0).then_inc(dinv_ready, 1)
            engine.wait_ge(dinv_ready, j + 1)
            scaled(dinv_half[:, c], dinv[:, c], 0.5, 0.0).then_inc(half_ready, 1)

        def block(ap, k):
            return ap[bass.ts(k, P), :]

        ctx_block = ctx.enter_context(nc.Block())

        @ctx_block.sync
        def _(sp):
            def load_x(k, s, slot):
                sp.dma_start(xr[:, slot, :], block(x, k)).then_inc(x_in[slot], 16)

            def load_ux(g, blocks):
                for m in blocks:
                    sp.dma_start(ux[:, m, :], block(x, m)).then_inc(ux_in[g], 16)

            def load_rows(j):
                if j >= RING_R:
                    sp.wait_ge(ml_done, j - RING_R + 1)
                if j == 0:
                    for n in range(PIECES):
                        cols = slice(n * N // PIECES, (n + 1) * N // PIECES)
                        sp.dma_start(strip_row[:, 0, cols], block(adj, 0)[:, cols]).then_inc(piece_in[n], 16)
                else:
                    sp.dma_start(strip_row[:, j % RING_R, :], block(adj, j)).then_inc(row_in[j % RING_R], 16)

            def load_cols(j):
                if j >= 2:
                    sp.wait_ge(tr_copied, BATCH_BASE[j - 1])
                size = BATCH if j == 0 else NB
                for n, r in enumerate(range(j + 1, NB, size)):
                    last = min(r + size, NB)
                    sp.dma_start(strip_col[:, j % 2, r - j - 1:last - j - 1, :],
                                 adj[r * P:last * P, j * P:(j + 1) * P].rearrange("(r p) c -> p r c", p=P)
                                 ).then_inc(col_in[j % 2] if j else piece_in[PIECES + n], 16)

            for j in range(RING_R):
                load_rows(j)
                if j < 3:
                    load_cols(j)
                if j < 2:
                    load_x(j, j, j)
            load_rows(RING_R)
            load_cols(3)
            for j in range(2, NB):
                if 2 < j < NB - 2:
                    load_rows(j + 2)
                sp.wait_ge(zl_done, j - 1)
                load_x(j, j, j % 2)
                if 1 < j and j + 2 < NB - 1:
                    load_cols(j + 2)
                if j == UX_STEP:
                    load_ux(0, GROUPS[0])

            def load_step(g, k, s, slot):
                sp.wait_ge(ml_done, s - 1)
                m0 = GROUPS[g][0]
                sp.dma_start(natural[slot][:, :], block(adj, k)[:, m0 * P:(m0 + G1) * P]
                             ).then_inc(nat_in[slot], 16)
                sp.wait_ge(zl_done, s - 1)
                load_x(k, s, slot)

            for g in (1, 2):
                load_step(g, 0, g * NB, 0)
                load_step(g, 1, g * NB + 1, 1)
                sp.wait_ge(tr_copied, BATCH_BASE[NB])
                load_ux(g, GROUPS[g])
                with sp.Fori(1, NB // 2) as i:
                    for slot in range(2):
                        load_step(g, 2 * i + slot, 2 * i + (g * NB + slot), slot)

            sp.wait_ge(zl_done, LAST1 - 1)
            load_x(0, 0, 0)
            sp.wait_ge(zl_done, LAST1)
            load_x(1, 0, 1)

            def store(m, slot):
                sp.wait_ge(o_ready, m + 1)
                sp.dma_start(block(out, m), outr[:, slot, :]).then_inc(out_done[slot], 16)

            with sp.Fori(0, NB // 2 - 1) as i:
                for slot in range(2):
                    store(2 * i + slot, slot)
                    load_x(2 * i + (2 + slot), 0, slot)
            for slot in range(2):
                store(NB - 2 + slot, slot)
            for slot in range(2):
                sp.wait_ge(out_done[slot], 16 * (NB // 2))

        @ctx_block.gpsimd
        def _(pool):
            nc.gpsimd.memset(ident[:, :], 0.0).then_inc(ident_ready, 1)
            pool.wait_ge(ident_ready, 1)
            nc.gpsimd.affine_select(out=ident[:, :], in_=ident[:, :], compare_op=ALU.not_equal, fill=1.0,
                                    base=0, pattern=[[-1, P]], channel_multiplier=1).then_inc(ident_ready, 1)

            def ex_scale(m):
                nc.gpsimd.tensor_scalar(ux[:, m, :], ux[:, m, :], dinv[:, m:m + 1], dinv[:, m:m + 1],
                                        ALU.mult, ALU.mult).then_inc(ex_done, 1)

            for g in range(3):
                pool.wait_ge(dinv_ready, GROUPS[g][-1] + 1)
                pool.wait_ge(ux_in[g], 16 * len(GROUPS[g]))
                for m in GROUPS[g]:
                    ex_scale(m)
                for m in GROUPS[g]:
                    pool.wait_ge(uh_done, m + 1)
                    nc.gpsimd.tensor_tensor(UL[:, m, :], ux[:, m, :], UH[:, m, :].bitcast(F32), ALU.subtract
                                            ).then_inc(ul_done, 1)

        @ctx_block.scalar
        def _(act):
            def copy_batch(j, n):
                kind, first, count = BATCHES[j][n]
                b = BATCH_BASE[j] + n
                act.wait_ge(tr_done, b + 1)
                src = TB[b % 2][:, 0:count * P]
                if kind == "col":
                    dst = AT[:, j, first * P:(first + count) * P]
                else:
                    dst = AT[:, first:first + count, j * P:(j + 1) * P]
                    src = src.rearrange("p (n c) -> p n c", n=count)
                nc.scalar.activation(dst, src, ACT.Copy).then_inc(tr_copied, 1)

            def z_high(k, s, slot):
                act.wait_ge(x_in[slot], nth(s, slot))
                nc.scalar.activation(ZH[slot][:, :], xr[:, slot, :], ACT.Copy, scale=dinv[:, bass.ds(k, 1)]
                                     ).then_inc(zh_done, 1)

            def u_high(blocks):
                for m in blocks:
                    act.wait_ge(u_done, m + 1)
                    nc.scalar.activation(UH[:, m, :], ux[:, m, :], ACT.Copy).then_inc(uh_done, 1)

            def degree_root(j):
                act.wait_ge(degc_ready, j + 1)
                nc.scalar.activation(root[:, j:j + 1], degc[:, j:j + 1], ACT.Sqrt).then_inc(root_done, 1)

            def scaled(out, in_, scale, bias):
                return nc.scalar.activation(out, in_, ACT.Copy, scale=scale, bias=bias)

            act.wait_ge(ident_ready, 2)
            nc.scalar.activation(spare[:, :], ident[:, 0:1], ACT.Sqrt)
            for n in range(len(BATCHES[0])):
                copy_batch(0, n)
            for j in range(NB):
                todo = between_products(j - 1) if j else [(1, n) for n in range(len(BATCHES[1]))]
                if j <= AHEAD:
                    for i, n in todo[:COPIES_FOR_SUM[j]]:
                        copy_batch(i, n)
                    todo = todo[COPIES_FOR_SUM[j]:]
                if j <= AHEAD:
                    degree_root(j)
                if j >= 2:
                    act.wait_ge(prod_done, through(0, j - 2))
                act.wait_ge(msum_done, j + 1)
                nc.scalar.activation(MH[j % 2][:, :], strip_row[:, j % RING_R, 0:GW], ACT.Copy
                                     ).then_inc(mh_done, 1)
                for i, n in todo[:COPIES_FOR_D[min(j, AHEAD + 1)]]:
                    copy_batch(i, n)
                todo = todo[COPIES_FOR_D[min(j, AHEAD + 1)]:]
                act.wait_ge(dinv_ready, j + 1)
                z_high(j, j, j % 2)
                few = len(todo) // 4
                for i, n in todo[:few]:
                    copy_batch(i, n)
                if AHEAD <= j < NB - 1:
                    degree_root(j + 1)
                for i, n in todo[few:]:
                    copy_batch(i, n)
                if AHEAD <= j < NB - 1:
                    degree(j + 1, act, scaled)

            def split_high(g, k, s, slot, before):
                act.wait_ge(prod_done, before)
                z_high(k, s, slot)
                act.wait_ge(msum_done, s + 1)
                nc.scalar.activation(MH[slot][:, 0:G1 * P], natural[slot][:, :], ACT.Copy
                                     ).then_inc(mh_done, 1)

            for g in (1, 2):
                split_high(g, 0, g * NB, 0, through(g - 1, NB - 2))
                u_high(GROUPS[g - 1][:3])
                split_high(g, 1, g * NB + 1, 1, through(g - 1, NB - 1))
                u_high(GROUPS[g - 1][3:])
                with act.Fori(1, NB // 2) as i:
                    for slot in range(2):
                        split_high(g, 2 * i + slot, 2 * i + (g * NB + slot), slot,
                                   2 * WIDTHS[g] * i + through(g, slot - 2))

            def half_high(m, h):
                nc.scalar.activation(ATH[h][:, :, :], AT[:, h * HALF:(h + 1) * HALF, bass.ts(m, P)], ACT.Copy
                                     ).then_inc(ath_done, 1)

            def ln_root(m, slot):
                act.wait_ge(var_ready, m + 1)
                nc.scalar.activation(ln[:, slot, 1:2], ln[:, slot, 0:1], ACT.Sqrt).then_inc(lroot_done, 1)

            act.wait_ge(prod_done, through(2, NB - 2))
            half_high(0, 0)
            u_high(GROUPS[2])
            act.wait_ge(prod_done, PAIRS[3])
            half_high(0, 1)

            def columns_high(m, prev_slot):
                for h in range(2):
                    act.wait_ge(half_done, 2 * m + (h - 1))
                    half_high(m, h)
                ln_root(m - 1, prev_slot)

            columns_high(1, 0)
            with act.Fori(1, NB // 2) as i:
                for slot in range(2):
                    columns_high(2 * i + slot, 1 - slot)
            ln_root(NB - 1, 1)

        @ctx_block.vector
        def _(dve):
            def m_low(width, src, s, slot):
                dve.wait_ge(mh_done, s + 1)
                nc.vector.tensor_tensor(ML[slot][:, 0:width], src, MH[slot][:, 0:width].bitcast(F32),
                                        ALU.subtract).then_inc(ml_done, 1)

            def z_low(k, s, slot):
                dve.wait_ge(zh_done, s + 1)
                nc.vector.scalar_tensor_tensor(out=ZL[slot][:, :], in0=xr[:, slot, :],
                                               scalar=dinv[:, bass.ds(k, 1)],
                                               in1=ZH[slot][:, :].bitcast(F32),
                                               op0=ALU.mult, op1=ALU.subtract).then_inc(zl_done, 1)

            def row_sums(j):
                strip, c = strip_row[:, j % RING_R, :], slice(j, j + 1)

                def add_transposed(cols, total):
                    return nc.vector.scalar_tensor_tensor(out=strip[:, cols], in0=strip[:, cols], scalar=1.0,
                                                          in1=AT[:, j, cols], op0=ALU.mult, op1=ALU.add,
                                                          accum_out=total)

                if j >= PIECEWISE:
                    dve.wait_ge(tr_copied, BATCH_BASE[j + 1])
                    dve.wait_ge(row_in[j % RING_R], row_nth(j))
                    add_transposed(slice(0, N), rowsum[:, c]).then_inc(msum_done, 1)
                    dve.wait_ge(msum_done, j + 1)
                    return
                cuts = [0] + [r for kind, r, _ in BATCHES[j] if kind == "col"][1:] + [NB]
                rows = sum(kind == "row" for kind, _, _ in BATCHES[j])
                if j > 0:
                    dve.wait_ge(row_in[j % RING_R], row_nth(j))
                for n, (p, q) in enumerate(zip(cuts, cuts[1:])):
                    dve.wait_ge(tr_copied, BATCH_BASE[j] + rows + n + 1)
                    add_transposed(slice(p * P, q * P), partial[:, n:n + 1]).then_inc(partial_done, 1)
                dve.wait_ge(partial_done, PARTS[j + 1])
                nc.vector.reduce_sum(rowsum[:, c], partial[:, 0:len(cuts) - 1], mybir.AxisListType.X
                                     ).then_inc(msum_done, 1)
                dve.wait_ge(msum_done, j + 1)

            def sums_to_degrees(j):
                c = slice(j, j + 1)
                nc.vector.tensor_scalar(deg[:, c], rowsum[:, c], 0.5, 1.0, ALU.mult, ALU.add).then_inc(deg_done, 1)
                dve.wait_ge(deg_done, j + 1)
                nc.vector.tensor_scalar(degc[:, c], deg[:, c], DEG_MIN, None, ALU.max).then_inc(degc_ready, 1)
                nc.vector.tensor_scalar(deg_neg[:, c], deg[:, c], DEG_MIN, -0.5, ALU.max, ALU.mult)
                nc.vector.tensor_scalar(mask[:, c], deg[:, c], 0.0, None, ALU.is_gt)

            def scaled(out, in_, scale, bias):
                return nc.vector.tensor_scalar(out, in_, scale, bias, ALU.mult, ALU.add)

            def invert_root(j):
                dve.wait_ge(root_done, j + 1)
                nc.vector.reciprocal(inv[:, j:j + 1], root[:, j:j + 1]).then_inc(inv_done, 1)

            for j in range(NB):
                if j <= AHEAD:
                    row_sums(j)
                    sums_to_degrees(j)
                    invert_root(j)
                    degree(j, dve, scaled)
                ahead = AHEAD <= j < NB - 1
                if ahead:
                    row_sums(j + 1)
                    sums_to_degrees(j + 1)
                m_low(GW, strip_row[:, j % RING_R, 0:GW], j, j % 2)
                z_low(j, j, j % 2)
                if ahead:
                    invert_root(j + 1)

            def finish_u(g, blocks):
                for m in blocks:
                    dve.wait_ge(prod_done, complete(g, m))
                    dve.wait_ge(ex_done, m + 1)
                    nc.vector.scalar_tensor_tensor(out=ux[:, m, :], in0=acc(m)[:, :], scalar=dinv_half[:, m:m + 1],
                                                   in1=ux[:, m, :], op0=ALU.mult, op1=ALU.add).then_inc(u_done, 1)

            def split_low(g, k, s, slot):
                m0 = GROUPS[g][0]
                dve.wait_ge(nat_in[slot], nth(s, slot) - 8 * NB)
                nc.vector.tensor_tensor(natural[slot][:, :], natural[slot][:, :],
                                        AT[:, bass.ds(k, 1), m0 * P:(m0 + G1) * P].rearrange("p o c -> p (o c)"),
                                        ALU.add).then_inc(msum_done, 1)
                z_low(k, s, slot)
                m_low(G1 * P, natural[slot][:, :], s, slot)

            dve.wait_ge(half_ready, NB)
            for g in (1, 2):
                split_low(g, 0, g * NB, 0)
                finish_u(g - 1, GROUPS[g - 1][:4])
                split_low(g, 1, g * NB + 1, 1)
                finish_u(g - 1, GROUPS[g - 1][4:])
                with dve.Fori(1, NB // 2) as i:
                    for slot in range(2):
                        split_low(g, 2 * i + slot, 2 * i + (g * NB + slot), slot)

            def half_low(m, h):
                dve.wait_ge(ath_done, 2 * m + (h + 1))
                nc.vector.tensor_tensor(ATL[h][:, :, :], AT[:, h * HALF:(h + 1) * HALF, bass.ts(m, P)],
                                        ATH[h][:, :, :].bitcast(F32), ALU.subtract).then_inc(atl_done, 1)

            LN_LINKS = 6

            def layer_norm(m, slot, first):
                def link(ins, n):
                    ins.then_inc(ln_chain, 1)
                    dve.wait_ge(ln_chain, LN_LINKS * m + n)

                veps, root_, inv_, c1, c2, rstd = (ln[:, slot, n:n + 1] for n in range(6))
                r = xr[:, slot, :]
                dve.wait_ge(half_done, 2 * m + 2)
                dve.wait_ge(x_in[slot], nth(m, slot) + 8 * LAST1)
                nc.vector.tensor_tensor(r, banks[slot][:, :], r, ALU.add).then_inc(y_read, 1)
                dve.wait_ge(y_read, m + 1)
                link(nc.vector.bn_stats(stats[:, slot, :], r), 1)
                nc.vector.memset(veps, LN_EPS)
                link(nc.vector.bn_aggr(meanvar[:, slot, :], stats[:, slot, :]), 2)
                nc.vector.tensor_tensor(veps, meanvar[:, slot, 1:2], veps, ALU.add).then_inc(var_ready, 1)
                dve.wait_ge(lroot_done, m + 1)
                link(nc.vector.reciprocal(inv_, root_), 3)
                link(nc.vector.scalar_tensor_tensor(out=c1, in0=inv_, scalar=veps, in1=inv_,
                                                    op0=ALU.mult, op1=ALU.mult), 4)
                link(nc.vector.tensor_scalar(c2, c1, -0.5, 1.5, ALU.mult, ALU.add), 5)
                link(nc.vector.tensor_scalar(rstd, inv_, c2, None, ALU.mult), 6)
                if not first:
                    dve.wait_ge(out_done[slot], 8 * m - 8 * slot)
                nc.vector.tensor_scalar(outr[:, slot, :], r, meanvar[:, slot, 0:1], rstd, ALU.subtract, ALU.mult
                                        ).then_inc(o_ready, 1)

            half_low(0, 0)
            finish_u(2, GROUPS[2])
            half_low(0, 1)
            for m in (1, 2, 3):
                half_low(m, 0)
                half_low(m, 1)
                layer_norm(m - 1, (m - 1) % 2, first=m < 3)
            with dve.Fori(2, NB // 2) as i:
                for slot in range(2):
                    half_low(2 * i + slot, 0)
                    half_low(2 * i + slot, 1)
                    layer_norm(2 * i + (slot - 1), 1 - slot, first=False)
            layer_norm(NB - 1, 1, first=False)

        @ctx_block.tensor
        def _(pe):
            def transpose_batch(j, n):
                kind, first, count = BATCHES[j][n]
                b = BATCH_BASE[j] + n
                if j == 0 and kind == "row":
                    pe.wait_ge(piece_in[first // BATCH], 16)
                elif n == 0:
                    pe.wait_ge(row_in[j % RING_R], row_nth(j))
                if j == 0 and kind == "col":
                    pe.wait_ge(piece_in[PIECES + (first - 1) // BATCH], 16)
                elif kind == "col" and first == j + 1:
                    pe.wait_ge(col_in[j % 2], col_nth(j))
                if b >= 2:
                    pe.wait_ge(tr_copied, b - 1)
                for i in range(count):
                    if kind == "row":
                        src = strip_row[:, j % RING_R, (first + i) * P:(first + i + 1) * P]
                    else:
                        src = strip_col[:, j % 2, first + i - j - 1, :]
                    last = nc.tensor.transpose(TB[b % 2][:, i * P:(i + 1) * P], src, ident[:, :])
                last.then_inc(tr_done, 1)

            def products(bank, wh, wl, mh, ml, start, stop):
                nc.tensor.matmul(bank, wh, ml, start=start, stop=False)
                nc.tensor.matmul(bank, wl, mh, start=False, stop=False)
                return nc.tensor.matmul(bank, wh, mh, start=False, stop=stop)

            def contract(group, s, slot, start=False, stop=False, between=None):
                pe.wait_ge(ml_done, s + 1)
                pe.wait_ge(zl_done, s + 1)
                for n, m in enumerate(group):
                    if start and m >= 8:
                        pe.wait_ge(u_done, m - 7)
                    cols = slice(n * P, (n + 1) * P)
                    last = products(acc(m)[:, :], MH[slot][:, cols], ML[slot][:, cols],
                                    ZH[slot][:, :], ZL[slot][:, :], start, stop)
                    last.then_inc(prod_done, 1)
                    if between:
                        between(n)

            pe.wait_ge(ident_ready, 2)
            for n in range(len(BATCHES[0])):
                transpose_batch(0, n)
            for n in range(len(BATCHES[1])):
                transpose_batch(1, n)
            for j in range(NB):
                todo = between_products(j)
                first = FIRST_ROUND[min(j, AHEAD)]
                span = len(GROUPS[0]) - first
                cuts = [q * len(todo) // span for q in range(span + 1)]
                rounds = [[]] * first + [todo[p:q] for p, q in zip(cuts, cuts[1:])]

                def between(n):
                    for i, q in rounds[n]:
                        transpose_batch(i, q)

                contract(GROUPS[0], j, j % 2, start=j == 0, stop=j == NB - 1, between=between)

            pe.wait_ge(tr_copied, BATCH_BASE[NB])
            for g in (1, 2):
                group = GROUPS[g]
                contract(group, g * NB, 0, start=True)
                with pe.Fori(0, NB // 2 - 1) as i:
                    for n, slot in ((1, 1), (2, 0)):
                        contract(group, 2 * i + (g * NB + n), slot)
                contract(group, (g + 1) * NB - 1, 1, stop=True)

            def column(m, slot, first=False):
                for h in range(2):
                    pe.wait_ge(atl_done, 2 * m + (h + 1))
                    for n in range(HALF):
                        k = h * HALF + n
                        if first:
                            pe.wait_ge(ul_done, k + 1)
                        last = products(banks[slot][:, :], ATH[h][:, n, :], ATL[h][:, n, :],
                                        UH[:, k, :], UL[:, k, :], k == 0, k == NB - 1)
                    last.then_inc(half_done, 1)

            pe.wait_ge(u_done, GROUPS[2][0] - 1)
            column(0, 0, first=True)
            column(1, 1)
            with pe.Fori(1, NB // 2) as i:
                for slot in range(2):
                    pe.wait_ge(y_read, 2 * i + (slot - 1))
                    column(2 * i + slot, slot)


def kernel(x, adj):
    import numpy as np
    import concourse.bacc as bacc
    from concourse.bass_utils import run_bass_kernel_spmd

    nc = bacc.Bacc("TRN2", target_bir_lowering=False, num_devices=1, dynamic_dma_scratch_size=1024)
    arrays, args = {}, []
    for name, a in (("x", x), ("adj", adj)):
        a = np.ascontiguousarray(a)
        arrays[f"in_{name}"] = a
        args.append(nc.dram_tensor(f"in_{name}", a.shape, mybir.dt.from_np(a.dtype), kind="ExternalInput").ap())
    args.append(nc.dram_tensor("out_0", x.shape, F32, kind="ExternalOutput").ap())
    gnn_resnorm_kernel(nc, *args)
    r = run_bass_kernel_spmd(nc, [arrays], core_ids=[0])
    return r.results[0]["out_0"]
```
